# Optimizing a Trainium2 kernel written in Bass

```python
import numpy as np
import jax
import jax.numpy as jnp

def _softmax(x, axis=-1):
    return jax.nn.softmax(x, axis=axis)

def _gelu(x):
    return jax.nn.gelu(x, approximate=True)

def _silu(x):
    return jax.nn.silu(x)

def _sigmoid(x):
    return jax.nn.sigmoid(x)

def _layernorm(x, axis=-1, eps=1e-05):
    m = jnp.mean(x, axis=axis, keepdims=True)
    v = jnp.var(x, axis=axis, keepdims=True)
    return (x - m) / jnp.sqrt(v + eps)

def _scatter_add(tgt, idx, src, axis=0):
    return tgt.at[idx].add(src)

def _segment_sum(src, seg, n):
    return jax.ops.segment_sum(src, seg, n)
kernel_name = 'mk_dlrm_tower_d1_rec_r8_507c0c'

def setup_inputs(seed: int=0):
    np.random.seed(seed)
    _w = jnp.asarray

    def _rec_inputs():
        import jax
        import jax.numpy as jnp
        _tk = jax.random.key(seed)
        ids = jnp.stack([jax.random.randint(jax.random.fold_in(_tk, 200 + f), (2048,), 0, v, jnp.int32) for f, v in enumerate([1000, 1250, 125000, 1250, 1000, 1250, 12500, 1250, 12500, 12500, 12500, 12500, 1000, 1250, 12500, 1250, 1250, 1000, 1000, 12500, 12500, 1000, 1250, 1250, 1250, 1000])], axis=1)
        tbl_0 = 0.05 * jax.random.normal(jax.random.fold_in(_tk, 500 + 0), (1000, 128), jnp.float32)
        tbl_1 = 0.05 * jax.random.normal(jax.random.fold_in(_tk, 500 + 1), (1250, 128), jnp.float32)
        tbl_2 = 0.05 * jax.random.normal(jax.random.fold_in(_tk, 500 + 2), (125000, 128), jnp.float32)
        tbl_3 = 0.05 * jax.random.normal(jax.random.fold_in(_tk, 500 + 3), (1250, 128), jnp.float32)
        tbl_4 = 0.05 * jax.random.normal(jax.random.fold_in(_tk, 500 + 4), (1000, 128), jnp.float32)
        tbl_5 = 0.05 * jax.random.normal(jax.random.fold_in(_tk, 500 + 5), (1250, 128), jnp.float32)
        tbl_6 = 0.05 * jax.random.normal(jax.random.fold_in(_tk, 500 + 6), (12500, 128), jnp.float32)
        tbl_7 = 0.05 * jax.random.normal(jax.random.fold_in(_tk, 500 + 7), (1250, 128), jnp.float32)
        tbl_8 = 0.05 * jax.random.normal(jax.random.fold_in(_tk, 500 + 8), (12500, 128), jnp.float32)
        tbl_9 = 0.05 * jax.random.normal(jax.random.fold_in(_tk, 500 + 9), (12500, 128), jnp.float32)
        tbl_10 = 0.05 * jax.random.normal(jax.random.fold_in(_tk, 500 + 10), (12500, 128), jnp.float32)
        tbl_11 = 0.05 * jax.random.normal(jax.random.fold_in(_tk, 500 + 11), (12500, 128), jnp.float32)
        tbl_12 = 0.05 * jax.random.normal(jax.random.fold_in(_tk, 500 + 12), (1000, 128), jnp.float32)
        tbl_13 = 0.05 * jax.random.normal(jax.random.fold_in(_tk, 500 + 13), (1250, 128), jnp.float32)
        tbl_14 = 0.05 * jax.random.normal(jax.random.fold_in(_tk, 500 + 14), (12500, 128), jnp.float32)
        tbl_15 = 0.05 * jax.random.normal(jax.random.fold_in(_tk, 500 + 15), (1250, 128), jnp.float32)
        tbl_16 = 0.05 * jax.random.normal(jax.random.fold_in(_tk, 500 + 16), (1250, 128), jnp.float32)
        tbl_17 = 0.05 * jax.random.normal(jax.random.fold_in(_tk, 500 + 17), (1000, 128), jnp.float32)
        tbl_18 = 0.05 * jax.random.normal(jax.random.fold_in(_tk, 500 + 18), (1000, 128), jnp.float32)
        tbl_19 = 0.05 * jax.random.normal(jax.random.fold_in(_tk, 500 + 19), (12500, 128), jnp.float32)
        tbl_20 = 0.05 * jax.random.normal(jax.random.fold_in(_tk, 500 + 20), (12500, 128), jnp.float32)
        tbl_21 = 0.05 * jax.random.normal(jax.random.fold_in(_tk, 500 + 21), (1000, 128), jnp.float32)
        tbl_22 = 0.05 * jax.random.normal(jax.random.fold_in(_tk, 500 + 22), (1250, 128), jnp.float32)
        tbl_23 = 0.05 * jax.random.normal(jax.random.fold_in(_tk, 500 + 23), (1250, 128), jnp.float32)
        tbl_24 = 0.05 * jax.random.normal(jax.random.fold_in(_tk, 500 + 24), (1250, 128), jnp.float32)
        tbl_25 = 0.05 * jax.random.normal(jax.random.fold_in(_tk, 500 + 25), (1000, 128), jnp.float32)
        _rk = jax.random.fold_in(_tk, 7)
        r_dense_x = -0.000514642 + 1.00011 * jax.random.normal(jax.random.fold_in(_rk, 101), (2048, 128), jnp.float32)
        W_top1 = 0.0456912 * jax.random.normal(jax.random.fold_in(_tk, 801), (479, 512), jnp.float32)
        W_top2 = 0.0441942 * jax.random.normal(jax.random.fold_in(_tk, 802), (512, 256), jnp.float32)
        W_top3 = 0.0625 * jax.random.normal(jax.random.fold_in(_tk, 803), (256, 1), jnp.float32)
        b_top1 = jnp.zeros((512,), jnp.float32)
        b_top2 = jnp.zeros((256,), jnp.float32)
        return (r_dense_x, ids, tbl_0, tbl_1, tbl_2, tbl_3, tbl_4, tbl_5, tbl_6, tbl_7, tbl_8, tbl_9, tbl_10, tbl_11, tbl_12, tbl_13, tbl_14, tbl_15, tbl_16, tbl_17, tbl_18, tbl_19, tbl_20, tbl_21, tbl_22, tbl_23, tbl_24, tbl_25, W_top1, b_top1, W_top2, b_top2, W_top3)
    r_dense_x, ids, tbl_0, tbl_1, tbl_2, tbl_3, tbl_4, tbl_5, tbl_6, tbl_7, tbl_8, tbl_9, tbl_10, tbl_11, tbl_12, tbl_13, tbl_14, tbl_15, tbl_16, tbl_17, tbl_18, tbl_19, tbl_20, tbl_21, tbl_22, tbl_23, tbl_24, tbl_25, W_top1, b_top1, W_top2, b_top2, W_top3 = _rec_inputs()

    def _L0_rec_setup():
        import jax, jax.numpy as jnp
        import numpy as np
        F = 26
        D = 128
        B = 2048
        _TRIU_I, _TRIU_J = np.triu_indices(F + 1, k=1)
        _TRIU_I = jnp.asarray(_TRIU_I)
        _TRIU_J = jnp.asarray(_TRIU_J)
        key = jax.random.key(seed)
        k1, k2 = jax.random.split(key)
        sparse_x = jax.random.normal(k1, (B, F, D), dtype=jnp.float32)
        dense_x = jax.random.normal(k2, (B, D), dtype=jnp.float32)
        return {'sparse_x': sparse_x, 'dense_x': dense_x}
    _L0_rec_all = _L0_rec_setup()
    _L0_rec_in = {k: v for k, v in _L0_rec_all.items() if k in ()}
    del _L0_rec_all
    return {'r_dense_x': r_dense_x, 'ids': ids, 'tbl_0': tbl_0, 'tbl_1': tbl_1, 'tbl_2': tbl_2, 'tbl_3': tbl_3, 'tbl_4': tbl_4, 'tbl_5': tbl_5, 'tbl_6': tbl_6, 'tbl_7': tbl_7, 'tbl_8': tbl_8, 'tbl_9': tbl_9, 'tbl_10': tbl_10, 'tbl_11': tbl_11, 'tbl_12': tbl_12, 'tbl_13': tbl_13, 'tbl_14': tbl_14, 'tbl_15': tbl_15, 'tbl_16': tbl_16, 'tbl_17': tbl_17, 'tbl_18': tbl_18, 'tbl_19': tbl_19, 'tbl_20': tbl_20, 'tbl_21': tbl_21, 'tbl_22': tbl_22, 'tbl_23': tbl_23, 'tbl_24': tbl_24, 'tbl_25': tbl_25, 'W_top1': W_top1, 'b_top1': b_top1, 'W_top2': W_top2, 'b_top2': b_top2, 'W_top3': W_top3}

def reference(r_dense_x, ids, tbl_0, tbl_1, tbl_2, tbl_3, tbl_4, tbl_5, tbl_6, tbl_7, tbl_8, tbl_9, tbl_10, tbl_11, tbl_12, tbl_13, tbl_14, tbl_15, tbl_16, tbl_17, tbl_18, tbl_19, tbl_20, tbl_21, tbl_22, tbl_23, tbl_24, tbl_25, W_top1, b_top1, W_top2, b_top2, W_top3):
    import jax
    import jax.numpy as jnp

    def _L0_rec_ref(sparse_x, dense_x):
        import jax, jax.numpy as jnp
        import numpy as np
        F = 26
        D = 128
        B = 2048
        _TRIU_I, _TRIU_J = np.triu_indices(F + 1, k=1)
        _TRIU_I = jnp.asarray(_TRIU_I)
        _TRIU_J = jnp.asarray(_TRIU_J)
        combined = jnp.concatenate([sparse_x, dense_x[:, None, :]], axis=1)
        interact = jnp.einsum('bfd,bgd->bfg', combined, combined)
        return interact[:, _TRIU_I, _TRIU_J]
    e = jnp.stack([tbl_0[ids[:, 0]], tbl_1[ids[:, 1]], tbl_2[ids[:, 2]], tbl_3[ids[:, 3]], tbl_4[ids[:, 4]], tbl_5[ids[:, 5]], tbl_6[ids[:, 6]], tbl_7[ids[:, 7]], tbl_8[ids[:, 8]], tbl_9[ids[:, 9]], tbl_10[ids[:, 10]], tbl_11[ids[:, 11]], tbl_12[ids[:, 12]], tbl_13[ids[:, 13]], tbl_14[ids[:, 14]], tbl_15[ids[:, 15]], tbl_16[ids[:, 16]], tbl_17[ids[:, 17]], tbl_18[ids[:, 18]], tbl_19[ids[:, 19]], tbl_20[ids[:, 20]], tbl_21[ids[:, 21]], tbl_22[ids[:, 22]], tbl_23[ids[:, 23]], tbl_24[ids[:, 24]], tbl_25[ids[:, 25]]], axis=1)
    z = _L0_rec_ref(e, r_dense_x)
    z = z.reshape(z.shape[0], -1)
    h = jnp.concatenate([z, r_dense_x], axis=1)
    h = jnp.maximum(h @ W_top1 + b_top1, 0.0)
    h = jnp.maximum(h @ W_top2 + b_top2, 0.0)
    y = h @ W_top3
    return y

_drawn_inputs = setup_inputs


def setup_inputs(seed=0):
    import zlib

    import numpy as np

    out = dict(_drawn_inputs(seed))
    spreads = {'b_top1': (0.0, 0.1), 'b_top2': (0.0, 0.1)}
    factors = {}
    for name, (base, spread) in spreads.items():
        noise = np.random.default_rng([zlib.crc32(name.encode()), seed]).standard_normal(out[name].shape)
        drawn = base * np.exp(spread * noise) if base else spread * noise
        out[name] = jnp.asarray(drawn.astype(out[name].dtype))
    for name, factor in factors.items():
        out[name] = (out[name] * factor).astype(out[name].dtype)
    return out
```

```python
from contextlib import ExitStack

import concourse.bass as bass
from concourse import mybir

F32 = mybir.dt.float32
I32 = mybir.dt.int32
ALU = mybir.AluOpType
ACT = mybir.ActivationFunctionType

P = 128
ROWS = (1000, 1250, 125000, 1250, 1000, 1250, 12500, 1250, 12500, 12500, 12500, 12500, 1000,
        1250, 12500, 1250, 1250, 1000, 1000, 12500, 12500, 1000, 1250, 1250, 1250, 1000)
NF = len(ROWS)
FS = NF + 2
PER_BANK = 4
NGROUP = (NF + PER_BANK) // PER_BANK
NQ = 4
QUAD = P // NQ
GW = (NF + NQ - 1) // NQ
NSLOT = 2
H1, H2 = 512, 256
NH1, NH2 = H1 // P, H2 // P


def pair_rows():
    rows = [[-1] * GW for _ in range(P)]
    n = 0
    for f in range(NF + 1):
        for g in range(f + 1, NF + 1):
            q, j = divmod(g - 1, GW)
            rows[32 * q + f][j] = n
            n += 1
    return rows, n


def build(nc, ids, tables, dense, w1, b1, w2, b2, w3, ident, limit, out):
    batch = dense.shape[0]
    ntile = batch // P
    nblock = ntile // NSLOT
    BLK = NSLOT * P
    NSTEP = GW + 1

    with ExitStack() as ctx:
        def sb(name, shape, dt=F32):
            return ctx.enter_context(nc.sbuf_tensor(name, shape, dt))

        def psum(name, shape):
            return ctx.enter_context(nc.psum_tensor(name, shape, F32))

        def sem(name):
            return ctx.enter_context(nc.semaphore(name))

        ids_raw = sb("ids_raw", [P, ntile, NF], I32)
        ids_neg = sb("ids_neg", [P, ntile, NF], I32)
        ids_ok = sb("ids_ok", [P, ntile, NF], I32)
        lim = sb("lim", [P, NF], I32)
        idx = [sb(f"idx{s}", [P, NF], I32) for s in range(NSLOT)]
        emb = [sb(f"emb{s}", [P, NF + 1, P]) for s in range(NSLOT)]
        embT = [sb(f"embT{s}", [P, P, FS]) for s in range(NSLOT)]
        z = sb("z", [P, NSTEP, BLK])
        w1_sb = sb("w1_sb", [P, NSTEP, H1])
        w2_sb = sb("w2_sb", [P, NH1, H2])
        w3_sb = sb("w3_sb", [P, NH2])
        b1_sb = sb("b1_sb", [P, NH1])
        b2_sb = sb("b2_sb", [P, NH2])
        ident_sb = sb("ident_sb", [P, P])
        h1 = sb("h1", [P, NH1, BLK])
        h2 = sb("h2", [P, NH2, BLK])
        y = sb("y", [1, batch])

        tp = [psum(f"tp{k}", [P, PER_BANK, P]) for k in range(2)]
        zp = [psum(f"zp{s}", [P, QUAD, 32]) for s in range(NSLOT)]
        hp = [psum(f"hp{k}", [P, 512]) for k in range(2)]

        ids_in = sem("ids_in")
        weights_in = sem("weights_in")
        ident_in = sem("ident_in")
        clamp = sem("clamp")
        z_zero = sem("z_zero")
        idx_ready = [sem(f"idx_ready{s}") for s in range(NSLOT)]
        gathered = [[sem(f"gathered{s}_{g}") for g in range(NGROUP)] for s in range(NSLOT)]
        dense_in = [sem(f"dense_in{s}") for s in range(NSLOT)]
        transposed = [sem(f"transposed{s}") for s in range(NSLOT)]
        tp_full = [sem(f"tp_full{k}") for k in range(2)]
        tp_free = [sem(f"tp_free{k}") for k in range(2)]
        interacted = [sem(f"interacted{s}") for s in range(NSLOT)]
        z_ready = [sem(f"z_ready{s}") for s in range(NSLOT)]
        h1_full = sem("h1_full")
        h1_ready = sem("h1_ready")
        h2_full = sem("h2_full")
        h2_ready = sem("h2_ready")
        y_full = sem("y_full")
        y_ready = sem("y_ready")
        stored = sem("stored")

        def members(g):
            return range(PER_BANK * g, min(PER_BANK * (g + 1), NF + 1))

        def copies_before(s, g):
            return sum((NGROUP * s + g) % 2 == n % 2 for n in range(NGROUP * s + g))

        def copies_per_block(k):
            return sum(n % 2 == k for n in range(NGROUP * NSLOT))

        dense_v = dense.rearrange("(t p) d -> t p d", p=P)

        block = ctx.enter_context(nc.Block())

        @block.sync
        def _(sp):
            sp.dma_start(ids_raw[:], ids).then_inc(ids_in, 16)
            sp.dma_start(lim[:], limit).then_inc(ids_in, 16)
            sp.dma_start(w1_sb[:], w1).then_inc(weights_in, 16)

            def load_dense(s, i):
                sp.dma_start(emb[s][:, NF, :], dense_v[i * NSLOT + s, :, :]).then_inc(dense_in[s], 16)

            for s in range(NSLOT):
                load_dense(s, 0)
            with nc.sync.Fori(1, nblock) as i:
                for s in range(NSLOT):
                    sp.wait_ge(transposed[s], i)
                    load_dense(s, i)
            sp.wait_ge(y_ready, nblock)
            sp.dma_start(out.rearrange("b o -> o b"), y[:]).then_inc(stored, 16)
            sp.wait_ge(stored, 16)

        @block.gpsimd
        def _(pool):
            with nc.gpsimd.Fori(1, nblock + 1) as turn:
                for s in range(NSLOT):
                    pool.wait_ge(ids_in, 32)
                    pool.wait_ge(idx_ready[s], turn)
                    for f in range(NF):
                        nc.gpsimd.indirect_dma_start(
                            emb[s][:, f, :], None, tables[f],
                            bass.IndirectOffsetOnAxis(idx[s][:, f:f + 1], 0),
                        ).then_inc(gathered[s][f // PER_BANK], 16)

        @block.scalar
        def _(act):
            act.dma_start(ident_sb[:], ident).then_inc(ident_in, 16)
            act.dma_start(w2_sb[:], w2).then_inc(weights_in, 16)
            act.dma_start(w3_sb[:], w3).then_inc(weights_in, 16)
            act.dma_start(b1_sb[:], b1).then_inc(weights_in, 16)
            act.dma_start(b2_sb[:], b2).then_inc(weights_in, 16)

            def copy_tile(s, i, first=False):
                if not first:
                    act.wait_ge(z_ready[s], i)
                for g in range(NGROUP):
                    k = (NGROUP * s + g) % 2
                    m = members(g)
                    act.wait_ge(tp_full[k], i * copies_per_block(k) + (copies_before(s, g) + 1))
                    nc.scalar.copy(embT[s][:, :, m[0]:m[-1] + 1].rearrange("d b f -> d f b"),
                                   tp[k][:, 0:len(m), :]).then_inc(tp_free[k], 1)

            def mlp(j):
                for m in range(NH1):
                    act.wait_ge(h1_full, j * NH1 + (m + 1))
                    nc.scalar.activation(h1[:, m, :], hp[m % 2][:, 0:BLK], ACT.Relu,
                                         bias=b1_sb[:, m:m + 1]).then_inc(h1_ready, 1)
                for n in range(NH2):
                    act.wait_ge(h2_full, j * NH2 + (n + 1))
                    nc.scalar.activation(h2[:, n, :], hp[n % 2][:, 0:BLK], ACT.Relu,
                                         bias=b2_sb[:, n:n + 1]).then_inc(h2_ready, 1)
                act.wait_ge(y_full, j + 1)
                nc.scalar.copy(y[:, bass.ds(j * BLK, BLK)], hp[0][0:1, 0:BLK]).then_inc(y_ready, 1)

            copy_tile(0, 0, first=True)
            act.wait_ge(weights_in, 80)
            copy_tile(1, 0, first=True)
            with nc.scalar.Fori(1, nblock) as i:
                copy_tile(0, i)
                mlp(i - 1)
                copy_tile(1, i)
            mlp(nblock - 1)

        @block.vector
        def _(dve):
            dve.wait_ge(ids_in, 32)
            lim_b = lim[:, None, :].broadcast_to([P, ntile, NF])
            nc.vector.tensor_scalar(ids_neg[:], ids_raw[:], 0, None, ALU.is_lt).then_inc(clamp, 1)
            dve.wait_ge(clamp, 1)
            nc.vector.tensor_tensor(ids_neg[:], ids_neg[:], lim_b, ALU.mult).then_inc(clamp, 1)
            dve.wait_ge(clamp, 2)
            nc.vector.tensor_tensor(ids_ok[:], ids_raw[:], ids_neg[:], ALU.add).then_inc(clamp, 1)
            nc.vector.tensor_scalar(lim[:], lim[:], 1, None, ALU.subtract).then_inc(clamp, 1)
            dve.wait_ge(clamp, 4)
            nc.vector.tensor_tensor(ids_ok[:], ids_ok[:], lim_b, ALU.min).then_inc(clamp, 1)
            dve.wait_ge(clamp, 5)
            nc.vector.tensor_scalar(ids_ok[:], ids_ok[:], 0, None, ALU.max).then_inc(clamp, 1)
            dve.wait_ge(clamp, 6)

            nc.vector.memset(z[:], 0.0).then_inc(z_zero, 1)
            dve.wait_ge(z_zero, 1)

            def stage_indices(s, i):
                nc.vector.tensor_copy(idx[s][:], ids_ok[:, bass.ds(i * NSLOT + s, 1), :]
                                      ).then_inc(idx_ready[s], 1)

            def arrange_tile(s, i):
                dve.wait_ge(interacted[s], i + 1)
                for c in range(NQ):
                    for q in range(NQ):
                        w = min(GW, NF - GW * q)
                        nc.vector.tensor_copy(
                            z[32 * q:32 * q + NF, 0:w, P * s + QUAD * c:P * s + QUAD * (c + 1)],
                            zp[s][32 * c:32 * c + NF, :, GW * q:GW * q + w].rearrange("f u g -> f g u"))
                nc.vector.tensor_copy(z[:, GW, P * s:P * (s + 1)], embT[s][:, :, NF]
                                      ).then_inc(z_ready[s], 1)

            for s in range(NSLOT):
                stage_indices(s, 0)
            with nc.vector.Fori(0, nblock - 1) as i:
                for s in range(NSLOT):
                    dve.wait_ge(transposed[s], i + 1)
                    stage_indices(s, i + 1)
                    arrange_tile(s, i)
            for s in range(NSLOT):
                arrange_tile(s, nblock - 1)

        @block.tensor
        def _(pe):
            def transpose_tile(s, i, first=False):
                for g in range(NGROUP):
                    k = (NGROUP * s + g) % 2
                    m = members(g)
                    n = sum(f < NF for f in m)
                    pe.wait_ge(gathered[s][g], i * (16 * n) + 16 * n)
                    if m[-1] == NF:
                        pe.wait_ge(dense_in[s], i * 16 + 16)
                    if not first or copies_before(s, g):
                        pe.wait_ge(tp_free[k], i * copies_per_block(k) + copies_before(s, g))
                    for f in m:
                        last = nc.tensor.transpose(tp[k][:, f - m[0], :], emb[s][:, f, :], ident_sb[:])
                    last.then_inc(tp_full[k], 1)

            def interact_tile(s, i, after=None, first=False):
                for k in range(2):
                    done = copies_before(s, NGROUP - 1 - ((NGROUP * (s + 1) - 1) % 2 != k)) + 1
                    pe.wait_ge(tp_free[k], i * copies_per_block(k) + done)
                if not first:
                    pe.wait_ge(z_ready[s], i)
                for u in range(QUAD):
                    for c in range(NQ):
                        b = QUAD * c + u
                        last = nc.tensor.matmul(zp[s][32 * c:32 * c + NF, u, 0:NF],
                                                embT[s][:, b, 0:NF], embT[s][:, b, 1:NF + 1],
                                                start=True, stop=True)
                        if after is not None and u == c == 0:
                            last.then_inc(transposed[after], 1)
                last.then_inc(interacted[s], 1)

            def mlp(j, after=None):
                for s in range(NSLOT):
                    pe.wait_ge(z_ready[s], j + 1)
                for m in range(NH1):
                    if m >= 2:
                        pe.wait_ge(h1_ready, j * NH1 + (m - 1))
                    for k in range(NSTEP):
                        last = nc.tensor.matmul(hp[m % 2][:, 0:BLK], w1_sb[:, k, P * m:P * (m + 1)],
                                                z[:, k, :], start=(k == 0), stop=(k == NSTEP - 1))
                        if after is not None and m == k == 0:
                            last.then_inc(transposed[after], 1)
                    last.then_inc(h1_full, 1)
                for n in range(NH2):
                    for m in range(NH1):
                        if n == 0:
                            pe.wait_ge(h1_ready, j * NH1 + max(m + 1, NH1 - 1))
                        last = nc.tensor.matmul(hp[n % 2][:, 0:BLK], w2_sb[:, m, P * n:P * (n + 1)],
                                                h1[:, m, :], start=(m == 0), stop=(m == NH1 - 1))
                    last.then_inc(h2_full, 1)
                for n in range(NH2):
                    pe.wait_ge(h2_ready, j * NH2 + (n + 1))
                    last = nc.tensor.matmul(hp[0][0:1, 0:BLK], w3_sb[:, n:n + 1], h2[:, n, :],
                                            start=(n == 0), stop=(n == NH2 - 1))
                last.then_inc(y_full, 1)

            pe.wait_ge(ident_in, 16)
            transpose_tile(0, 0, first=True)
            interact_tile(0, 0, after=0, first=True)
            transpose_tile(1, 0, first=True)
            interact_tile(1, 0, after=1, first=True)
            pe.wait_ge(weights_in, 80)
            with nc.tensor.Fori(1, nblock) as i:
                transpose_tile(0, i)
                mlp(i - 1, after=0)
                interact_tile(0, i)
                transpose_tile(1, i)
                interact_tile(1, i, after=1)
                pe.wait_ge(y_ready, i)
            mlp(nblock - 1)


def kernel(**inputs):
    import numpy as np
    import concourse.bacc as bacc
    from concourse.bass_utils import run_bass_kernel_spmd

    ids = np.asarray(inputs["ids"])
    batch = ids.shape[0]
    w1 = np.asarray(inputs["W_top1"])
    rows, npair = pair_rows()
    w1_laid = np.zeros((P, GW + 1, H1), w1.dtype)
    for p in range(P):
        for j in range(GW):
            if rows[p][j] >= 0:
                w1_laid[p, j] = w1[rows[p][j]]
    w1_laid[:, GW] = w1[npair:]
    arrays = {
        "ids": np.ascontiguousarray(ids.reshape(batch // P, P, NF).transpose(1, 0, 2)),
        "dense": np.ascontiguousarray(inputs["r_dense_x"]),
        "w1": w1_laid,
        "b1": np.ascontiguousarray(np.asarray(inputs["b_top1"]).reshape(NH1, P).T),
        "w2": np.ascontiguousarray(np.asarray(inputs["W_top2"]).reshape(NH1, P, H2).transpose(1, 0, 2)),
        "b2": np.ascontiguousarray(np.asarray(inputs["b_top2"]).reshape(NH2, P).T),
        "w3": np.ascontiguousarray(np.asarray(inputs["W_top3"]).reshape(NH2, P).T),
        "ident": np.eye(P, dtype=np.float32),
        "limit": np.ascontiguousarray(np.broadcast_to(np.array(ROWS, np.int32), (P, NF))),
    }
    for f in range(NF):
        arrays[f"tbl_{f}"] = np.ascontiguousarray(inputs[f"tbl_{f}"])

    nc = bacc.Bacc("TRN2", target_bir_lowering=False, num_devices=1)
    ap = {name: nc.dram_tensor(name, a.shape, mybir.dt.from_np(a.dtype), kind="ExternalInput").ap()
          for name, a in arrays.items()}
    out = nc.dram_tensor("out", (batch, 1), F32, kind="ExternalOutput").ap()
    build(nc, ap["ids"], [ap[f"tbl_{f}"] for f in range(NF)], ap["dense"], ap["w1"], ap["b1"],
          ap["w2"], ap["b2"], ap["w3"], ap["ident"], ap["limit"], out)
    r = run_bass_kernel_spmd(nc, [arrays], core_ids=[0])
    return r.results[0]["out"]
```

```python
from contextlib import ExitStack

import concourse.bass as bass
from concourse import mybir

F32 = mybir.dt.float32
F32R = mybir.dt.float32r
I32 = mybir.dt.int32
ALU = mybir.AluOpType
ACT = mybir.ActivationFunctionType

P = 128
ROWS = (1000, 1250, 125000, 1250, 1000, 1250, 12500, 1250, 12500, 12500, 12500, 12500, 1000,
        1250, 12500, 1250, 1250, 1000, 1000, 12500, 12500, 1000, 1250, 1250, 1250, 1000)
NF = len(ROWS)
NHOT = 7
HOT = sorted(range(NF), key=lambda f: (ROWS[f], f))[:NHOT]
COLD = [f for f in range(NF) if f not in HOT]
NCOLD = len(COLD)
ORDER = COLD + [NF] + HOT
HROWS = ROWS[HOT[0]]
assert all(ROWS[f] == HROWS for f in HOT)
NCH = -(-HROWS // P)
HP = HROWS // NCH
assert HP * NCH == HROWS
FS = NF + 2
PER_BANK = 4
NGROUP = -(-(NCOLD + 1) // PER_BANK)
NQ = 4
QUAD = P // NQ
NSLOT = 2
NHB = 3
NPAIR = NF * (NF + 1) // 2
PSTEP = -(-NPAIR // P)
NSTEP = PSTEP + 1
H1, H2 = 512, 256
NH1, NH2 = H1 // P, H2 // P

HALVES = (
    ("M0", "T0", "I0", "M1", "T1", "I1", "Y", "T2", "I2", "T3", "I3", "A", "T4",
     "O0", "O1"),
    ("T0", "O2", "O3", "T1", "O4", "T2", "O5", "O6", "T3",
     "L0", "I0", "L1", "I1", "L2", "I2", "L3", "I3", "A", "T4"),
)
NPIECE = 4


def pair_groups():
    groups, last, p = [], NF, 0
    while last > 0:
        first = max(1, last - PSTEP + 1)
        groups.append((first, last, p))
        p += last
        last = first - 1
    assert p <= P
    return groups


GROUPS = pair_groups()


def fills_bank(step):
    return step[0] in "TO"


def build(nc, ids, ids_hot, tables, hot_tables, dense, dense_t, w1, b1, w2, b2, w3,
          ident, limit, hot_row, ids_scratch, out):
    batch = dense.shape[0]
    ntile = batch // P
    nblock = ntile // NSLOT
    BLK = NSLOT * P
    body = [(s, step) for s, half in enumerate(HALVES) for step in half]
    fills = [b for b in body if fills_bank(b[1])]
    assert len(fills) == 2 * NGROUP + NHOT and len(set(body)) == len(body)

    with ExitStack() as ctx:
        def sb(name, shape, dt=F32):
            return ctx.enter_context(nc.sbuf_tensor(name, shape, dt))

        def psum(name, shape):
            return ctx.enter_context(nc.psum_tensor(name, shape, F32))

        def sem(name):
            return ctx.enter_context(nc.semaphore(name))

        ids_raw = sb("ids_raw", [P, ntile, NCOLD], I32)
        ids_neg = sb("ids_neg", [P, ntile, NCOLD], I32)
        ids_ok = sb("ids_ok", [P, ntile, NCOLD], I32)
        lim = sb("lim", [P, NCOLD], I32)
        hot_raw = sb("hot_raw", [P, NHOT * batch // P], I32)
        hot_neg = sb("hot_neg", [P, NHOT * batch // P], I32)
        hot_ok = sb("hot_ok", [P, NHOT * batch // P], I32)
        hrow = sb("hrow", [HP, NCH], I32)
        hot_ids = sb("hot_ids", [HP, NHOT, BLK], I32)
        idx = [sb(f"idx{s}", [P, NCOLD], I32) for s in range(NSLOT)]
        emb = [sb(f"emb{s}", [P, NCOLD + 1, P]) for s in range(NSLOT)]
        embT = sb("embT", [P, BLK, FS])
        dots = sb("dots", [P, max(NF * BLK, NHOT * NCH * P)])
        dots_v = dots[0:NF, 0:NF * BLK].rearrange("p (b s) -> p b s", b=NF)
        raw_tab = dots[0:HP, 0:NHOT * NCH * P].rearrange("p (t c d) -> p t c d", t=NHOT, c=NCH)
        z = sb("z", [P, NSTEP, BLK])
        tab_hi = sb("tab_hi", [HP, NHOT, NCH, P], F32R)
        tab_lo = sb("tab_lo", [HP, NHOT, NCH, P], F32R)
        hot = [sb(f"hot{k}", [HP, NCH, BLK], F32R) for k in range(NHB)]
        w1_sb = sb("w1_sb", [P, NSTEP, H1])
        w2_sb = sb("w2_sb", [P, NH1, H2])
        w3_sb = sb("w3_sb", [P, NH2])
        b1_sb = sb("b1_sb", [P, NH1])
        b2_sb = sb("b2_sb", [P, NH2])
        ident_sb = sb("ident_sb", [P, P])
        h1 = sb("h1", [P, NH1, BLK])
        h2 = sb("h2", [P, NH2, BLK])
        y = sb("y", [P, ntile])

        tp = [psum(f"tp{k}", [P, 512]) for k in range(2)]
        zp = [psum(f"zp{s}", [P, QUAD, 32]) for s in range(NSLOT)]
        hp = [psum(f"hp{k}", [P, 512]) for k in range(2)]

        ids_in = sem("ids_in")
        hot_in = sem("hot_in")
        ident_in = sem("ident_in")
        w_in = sem("w_in")
        table_in = [sem(f"table_in{t}") for t in range(NHOT)]
        table_hi = sem("table_hi")
        table_lo = sem("table_lo")
        clamped = sem("clamped")
        scratch_out = sem("scratch_out")
        z_zero = sem("z_zero")
        hot_ids_in = sem("hot_ids_in")
        idx_ready = [sem(f"idx_ready{s}") for s in range(NSLOT)]
        gathered = [[sem(f"gathered{s}_{g}") for g in range(NGROUP)] for s in range(NSLOT)]
        dense_in = [sem(f"dense_in{s}") for s in range(NSLOT)]
        tile_read = [sem(f"tile_read{s}") for s in range(NSLOT)]
        bank_full = [sem(f"bank_full{k}") for k in range(2)]
        bank_free = [sem(f"bank_free{k}") for k in range(2)]
        hot_made = sem("hot_made")
        hot_done = sem("hot_done")
        interacted = [sem(f"interacted{s}") for s in range(NSLOT)]
        dots_v_out = [sem(f"dots_by_vector{s}") for s in range(NSLOT)]
        dots_s_out = [sem(f"dots_by_scalar{s}") for s in range(NSLOT)]
        z_in = [sem(f"z_in{s}") for s in range(NSLOT)]
        h1_full = sem("h1_full")
        h1_ready = sem("h1_ready")
        h2_full = sem("h2_full")
        h2_ready = sem("h2_ready")
        y_full = sem("y_full")
        y_ready = sem("y_ready")
        stored = sem("stored")

        def members(g):
            return range(PER_BANK * g, min(PER_BANK * (g + 1), NCOLD + 1))

        def cold_members(g):
            return sum(f < NCOLD for f in members(g))

        def on_bank_full(step):
            return step[0] == "T" and step != f"T{NGROUP - 1}"

        def fill_number(s, step):
            return fills.index((s, step))

        def bank_of(s, step):
            return fill_number(s, step) % 2

        def freed_before(s, step):
            n = fill_number(s, step)
            return sum(m % 2 == n % 2 for m in range(n))

        def freed_per_turn(k):
            return sum(m % 2 == k for m in range(len(fills)))

        def full_upto(s, step):
            n = fill_number(s, step)
            return sum(m % 2 == n % 2 and on_bank_full(fills[m][1]) for m in range(n + 1))

        def full_per_turn(k):
            return sum(m % 2 == k and on_bank_full(fills[m][1]) for m in range(len(fills)))

        Z_MOVES = (len(GROUPS) + 1, len(GROUPS))

        dense_v = dense.rearrange("(t p) d -> t p d", p=P)
        block = ctx.enter_context(nc.Block())

        @block.sync
        def _(sp):
            sp.dma_start(ids_raw[:], ids).then_inc(ids_in, 16)
            sp.dma_start(lim[:], limit).then_inc(ids_in, 16)
            sp.dma_start(hrow[:], hot_row).then_inc(hot_in, 16)

            def load_dense(s, i):
                sp.dma_start(emb[s][:, NCOLD, :], dense_v[i * NSLOT + s, :, :]).then_inc(dense_in[s], 16)

            def load_hot_ids(i):
                src = ids_scratch.rearrange("p n -> (p n)").rearrange("(t b) -> t b", t=NHOT)[
                    :, bass.ds(i * BLK, BLK)]
                sp.dma_start(hot_ids[:], src[None, :, :].broadcast_to([HP, NHOT, BLK])
                             ).then_inc(hot_ids_in, 16)

            def move_dots(s, j, first=False):
                if s == 0 and not first:
                    sp.wait_ge(h1_full, j * NH1)
                sp.wait_ge(dots_v_out[s], j + 1)
                sp.wait_ge(dots_s_out[s], j + 1)
                for lo, hi, p in GROUPS:
                    sp.dma_start(z[p:p + hi, 0:hi - lo + 1, P * s:P * (s + 1)],
                                 dots_v[0:hi, lo - 1:hi, P * s:P * (s + 1)]).then_inc(z_in[s], 16)
                if s == 0:
                    sp.dma_start(z[:, NSTEP - 1, :], dense_t[:, bass.ds(j * BLK, BLK)]).then_inc(z_in[s], 16)

            def turn(i, first=False, last=False):
                if not first:
                    move_dots(1, i - 1)
                if not last:
                    sp.wait_ge(hot_made, i * NHOT + NHOT)
                    load_hot_ids(i + 1)
                    sp.wait_ge(tile_read[0], i + 1)
                    load_dense(0, i + 1)
                move_dots(0, i, first)
                if not last:
                    sp.wait_ge(tile_read[1], i + 1)
                    load_dense(1, i + 1)

            for s in range(NSLOT):
                load_dense(s, 0)
            sp.wait_ge(clamped, 9)
            sp.dma_start(ids_scratch, hot_ok[:]).then_inc(scratch_out, 16)
            sp.wait_ge(scratch_out, 16)
            load_hot_ids(0)
            sp.wait_ge(z_zero, 1)
            turn(0, first=True)
            with nc.sync.Fori(1, nblock - 1) as i:
                turn(i)
            turn(nblock - 1, last=True)
            move_dots(1, nblock - 1)
            sp.wait_ge(y_ready, nblock)
            sp.dma_start(out, y[:]).then_inc(stored, 16)
            sp.wait_ge(stored, 16)

        @block.gpsimd
        def _(pool):
            with nc.gpsimd.Fori(1, nblock + 1) as turn:
                for s in range(NSLOT):
                    pool.wait_ge(ids_in, 32)
                    pool.wait_ge(idx_ready[s], turn)
                    for n in range(NCOLD):
                        nc.gpsimd.indirect_dma_start(
                            emb[s][:, n, :], None, tables[COLD[n]],
                            bass.IndirectOffsetOnAxis(idx[s][:, n:n + 1], 0),
                        ).then_inc(gathered[s][n // PER_BANK], 16)

        def dots_copy(copy, s, c):
            return copy(dots_v[:, :, P * s + QUAD * c:P * s + QUAD * (c + 1)],
                        zp[s][32 * c:32 * c + NF, :, 0:NF].rearrange("a u b -> a b u"))

        @block.scalar
        def _(act):
            act.dma_start(ident_sb[:], ident).then_inc(ident_in, 16)
            act.dma_start(hot_raw[:], ids_hot).then_inc(hot_in, 16)
            for t in range(NHOT):
                act.dma_start(raw_tab[:, t, :, :], hot_tables[t].rearrange("(p c) d -> p c d", c=NCH)
                              ).then_inc(table_in[t], 16)
            act.dma_start(w1_sb[:], w1).then_inc(w_in, 16)
            act.dma_start(w2_sb[:], w2).then_inc(w_in, 16)
            act.dma_start(w3_sb[:], w3).then_inc(w_in, 16)
            act.dma_start(b1_sb[:], b1).then_inc(w_in, 16)
            act.dma_start(b2_sb[:], b2).then_inc(w_in, 16)
            for t in range(NHOT):
                act.wait_ge(table_in[t], 16)
                nc.scalar.copy(tab_hi[:, t, :, :], raw_tab[:, t, :, :]).then_inc(table_hi, 1)

            def embT_cols(s, lo, hi):
                return embT[:, P * s:P * (s + 1), lo:hi].rearrange("d b f -> d f b")

            def empty_bank(s, step, i, first):
                k = bank_of(s, step)
                n = int(step[1:])
                if step[0] == "O":
                    act.wait_ge(hot_done, i * NHOT + (n + 1))
                elif on_bank_full(step):
                    act.wait_ge(bank_full[k], i * full_per_turn(k) + full_upto(s, step))
                else:
                    act.wait_ge(tile_read[s], i + 1)
                if step[0] == "T":
                    if n == 0 and not first:
                        act.wait_ge(interacted[s], i)
                    m = members(n)
                    src = tp[k][:, 0:P * len(m)].rearrange("d (f b) -> d f b", b=P)
                    nc.scalar.copy(embT_cols(s, m[0], m[-1] + 1), src).then_inc(bank_free[k], 1)
                else:
                    if n == 0 and not first:
                        act.wait_ge(interacted[1], i)
                    nc.scalar.copy(embT[:, :, NCOLD + 1 + n], tp[k][:, 0:BLK]).then_inc(bank_free[k], 1)

            def copy_dots(s, j):
                act.wait_ge(interacted[s], j + 1)
                dots_copy(nc.scalar.copy, s, 2)
                dots_copy(nc.scalar.copy, s, 3).then_inc(dots_s_out[s], 1)

            def first_layer(m, j):
                act.wait_ge(h1_full, j * NH1 + (m + 1))
                nc.scalar.activation(h1[:, m, :], hp[m % 2][:, 0:BLK], ACT.Relu,
                                     bias=b1_sb[:, m:m + 1]).then_inc(h1_ready, 1)

            def second_layer(n, j):
                act.wait_ge(h2_full, j * NH2 + (n + 1))
                nc.scalar.activation(h2[:, n, :], hp[n % 2][:, 0:BLK], ACT.Relu,
                                     bias=b2_sb[:, n:n + 1]).then_inc(h2_ready, 1)

            def output(j):
                act.wait_ge(y_full, j + 1)
                nc.scalar.copy(y[:, bass.ds(j * NSLOT, NSLOT)], hp[0][:, 0:NSLOT]).then_inc(y_ready, 1)

            def turn(i, before=2):
                first = before == 0
                for s, step in body:
                    n = int(step[1:] or 0)
                    if fills_bank(step):
                        empty_bank(s, step, i, first)
                    elif step == "A" and s == 0 and before >= 1:
                        copy_dots(1, i - 1)
                    elif step == "A" and s == 1:
                        copy_dots(0, i)
                    elif step[0] == "L" and before >= 1:
                        first_layer(n, i - 1)
                    elif step[0] == "M" and before >= 2:
                        second_layer(n, i - 2)
                    elif step == "Y" and before >= 2:
                        output(i - 2)

            act.wait_ge(table_lo, NHOT)
            turn(0, before=0)
            turn(1, before=1)
            with nc.scalar.Fori(2, nblock) as i:
                turn(i)
            copy_dots(1, nblock - 1)
            for n in range(NH2):
                second_layer(n, nblock - 2)
            output(nblock - 2)
            for m in range(NH1):
                first_layer(m, nblock - 1)
            for n in range(NH2):
                second_layer(n, nblock - 1)
            output(nblock - 1)

        @block.vector
        def _(dve):
            dve.wait_ge(ids_in, 32)
            lim_b = lim[:, None, :].broadcast_to([P, ntile, NCOLD])
            nc.vector.tensor_scalar(ids_neg[:], ids_raw[:], 0, None, ALU.is_lt).then_inc(clamped, 1)
            dve.wait_ge(clamped, 1)
            nc.vector.tensor_tensor(ids_neg[:], ids_neg[:], lim_b, ALU.mult).then_inc(clamped, 1)
            dve.wait_ge(clamped, 2)
            nc.vector.tensor_tensor(ids_ok[:], ids_raw[:], ids_neg[:], ALU.add).then_inc(clamped, 1)
            nc.vector.tensor_scalar(lim[:], lim[:], 1, None, ALU.subtract).then_inc(clamped, 1)
            dve.wait_ge(clamped, 4)
            nc.vector.tensor_tensor(ids_ok[:], ids_ok[:], lim_b, ALU.min).then_inc(clamped, 1)
            dve.wait_ge(clamped, 5)
            nc.vector.tensor_scalar(ids_ok[:], ids_ok[:], 0, None, ALU.max).then_inc(clamped, 1)
            dve.wait_ge(clamped, 6)

            def stage_indices(s, i):
                nc.vector.tensor_copy(idx[s][:], ids_ok[:, bass.ds(i * NSLOT + s, 1), :]
                                      ).then_inc(idx_ready[s], 1)

            for s in range(NSLOT):
                stage_indices(s, 0)
            dve.wait_ge(hot_in, 32)
            nc.vector.tensor_scalar(hot_neg[:], hot_raw[:], 0, HROWS, ALU.is_lt, ALU.mult).then_inc(clamped, 1)
            dve.wait_ge(clamped, 7)
            nc.vector.tensor_tensor(hot_ok[:], hot_raw[:], hot_neg[:], ALU.add).then_inc(clamped, 1)
            dve.wait_ge(clamped, 8)
            nc.vector.tensor_scalar(hot_ok[:], hot_ok[:], HROWS - 1, 0, ALU.min, ALU.max).then_inc(clamped, 1)

            nc.vector.memset(z[:], 0.0).then_inc(z_zero, 1)
            for t in range(NHOT):
                dve.wait_ge(table_hi, t + 1)
                nc.vector.tensor_tensor(tab_lo[:, t, :, :], raw_tab[:, t, :, :],
                                        tab_hi[:, t, :, :].bitcast(F32), ALU.subtract).then_inc(table_lo, 1)

            def make_hot(t, i, first):
                if t == 0:
                    dve.wait_ge(hot_ids_in, i * 16 + 16)
                if not first or t >= NHB:
                    dve.wait_ge(hot_done, i * NHOT + (t - NHB + 1))
                nc.vector.tensor_tensor(hot[(t % NHB)][:],
                                        hot_ids[:, t, :][:, None, :].broadcast_to([HP, NCH, BLK]),
                                        hrow[:, :, None].broadcast_to([HP, NCH, BLK]),
                                        ALU.is_equal).then_inc(hot_made, 1)

            def copy_dots(s, j):
                dve.wait_ge(interacted[s], j + 1)
                dots_copy(nc.vector.tensor_copy, s, 0)
                dots_copy(nc.vector.tensor_copy, s, 1).then_inc(dots_v_out[s], 1)

            def turn(i, first=False, last=False):
                for t in range(NHB):
                    make_hot(t, i, first)
                if not first:
                    copy_dots(1, i - 1)
                for t in range(NHB, NHOT):
                    make_hot(t, i, first)
                if not last:
                    dve.wait_ge(tile_read[0], i + 1)
                    stage_indices(0, i + 1)
                copy_dots(0, i)
                if not last:
                    dve.wait_ge(tile_read[1], i + 1)
                    stage_indices(1, i + 1)

            dve.wait_ge(table_lo, NHOT)
            turn(0, first=True)
            with nc.vector.Fori(1, nblock - 1) as i:
                turn(i)
            turn(nblock - 1, last=True)
            copy_dots(1, nblock - 1)

        @block.tensor
        def _(pe):
            def transpose_group(s, step, i, first):
                k, g = bank_of(s, step), int(step[1:])
                m = members(g)
                if cold := 16 * cold_members(g):
                    pe.wait_ge(gathered[s][g], i * cold + cold)
                if m[-1] == NCOLD:
                    pe.wait_ge(dense_in[s], i * 16 + 16)
                if not first or freed_before(s, step):
                    pe.wait_ge(bank_free[k], i * freed_per_turn(k) + freed_before(s, step))
                for f in m:
                    n = f - m[0]
                    last = nc.tensor.transpose(tp[k][:, P * n:P * (n + 1)], emb[s][:, f, :], ident_sb[:])
                last.then_inc(bank_full[k] if on_bank_full(step) else tile_read[s], 1)

            def hot_product(s, step, i, first):
                k, t = bank_of(s, step), int(step[1:])
                pe.wait_ge(hot_made, i * NHOT + (t + 1))
                if first:
                    pe.wait_ge(table_lo, t + 1)
                if not first or freed_before(s, step):
                    pe.wait_ge(bank_free[k], i * freed_per_turn(k) + freed_before(s, step))
                for c in range(NCH):
                    nc.tensor.matmul(tp[k][:, 0:BLK], tab_hi[:, t, c, :], hot[t % NHB][:, c, :],
                                     start=(c == 0), stop=False)
                    last = nc.tensor.matmul(tp[k][:, 0:BLK], tab_lo[:, t, c, :], hot[t % NHB][:, c, :],
                                            start=False, stop=(c == NCH - 1))
                last.then_inc(hot_done, 1)

            def interact(s, piece, j, first=False):
                if piece == 0:
                    for k in range(2):
                        upto = max(n for n in range(len(fills)) if n % 2 == k
                                   and (fills[n][0] == s or fills[n][1][0] == "O"))
                        done = sum(n % 2 == k for n in range(upto + 1))
                        pe.wait_ge(bank_free[k], j * freed_per_turn(k) + done)
                    if not first:
                        pe.wait_ge(dots_v_out[s], j)
                        pe.wait_ge(dots_s_out[s], j)
                n = QUAD // NPIECE
                for u in range(n * piece, n * (piece + 1)):
                    for c in range(NQ):
                        b = P * s + QUAD * c + u
                        last = nc.tensor.matmul(zp[s][32 * c:32 * c + NF, u, 0:NF],
                                                embT[:, b, 0:NF], embT[:, b, 1:NF + 1],
                                                start=True, stop=True)
                if piece == NPIECE - 1:
                    last.then_inc(interacted[s], 1)

            def first_layer(m, j):
                if m == 0:
                    for s in range(NSLOT):
                        pe.wait_ge(z_in[s], j * (16 * Z_MOVES[s]) + 16 * Z_MOVES[s])
                if m >= 2:
                    pe.wait_ge(h1_ready, j * NH1 + (m - 1))
                for k in range(NSTEP):
                    last = nc.tensor.matmul(hp[m % 2][:, 0:BLK], w1_sb[:, k, P * m:P * (m + 1)],
                                            z[:, k, :], start=(k == 0), stop=(k == NSTEP - 1))
                last.then_inc(h1_full, 1)

            def second_layer(n, j):
                if n == 0:
                    pe.wait_ge(h1_ready, j * NH1 + NH1)
                for m in range(NH1):
                    last = nc.tensor.matmul(hp[n % 2][:, 0:BLK], w2_sb[:, m, P * n:P * (n + 1)],
                                            h1[:, m, :], start=(m == 0), stop=(m == NH1 - 1))
                last.then_inc(h2_full, 1)

            def output(j):
                pe.wait_ge(h2_ready, j * NH2 + NH2)
                for s in range(NSLOT):
                    for n in range(NH2):
                        last = nc.tensor.matmul(hp[0][:, s:s + 1], h2[:, n, P * s:P * (s + 1)],
                                                w3_sb[:, n:n + 1], start=(n == 0), stop=(n == NH2 - 1))
                last.then_inc(y_full, 1)

            def turn(i, before=2):
                first = before == 0
                for s, step in body:
                    n = int(step[1:] or 0)
                    if step[0] == "T":
                        transpose_group(s, step, i, first)
                    elif step[0] == "O":
                        hot_product(s, step, i, first)
                    elif step[0] == "I" and s == 0 and before >= 1:
                        interact(1, n, i - 1, before == 1)
                    elif step[0] == "I" and s == 1:
                        interact(0, n, i, first)
                    elif step[0] == "L" and before >= 1:
                        first_layer(n, i - 1)
                    elif step[0] == "M" and before >= 2:
                        second_layer(n, i - 2)
                    elif step == "Y" and before >= 2:
                        output(i - 2)

            pe.wait_ge(ident_in, 16)
            turn(0, before=0)
            pe.wait_ge(w_in, 80)
            turn(1, before=1)
            with nc.tensor.Fori(2, nblock) as i:
                turn(i)
            for piece in range(NPIECE):
                interact(1, piece, nblock - 1)
            for n in range(NH2):
                second_layer(n, nblock - 2)
            output(nblock - 2)
            pe.wait_ge(y_ready, nblock - 1)
            for m in range(NH1):
                first_layer(m, nblock - 1)
            for n in range(NH2):
                second_layer(n, nblock - 1)
            output(nblock - 1)


def pair_row(f, g):
    return f * (2 * NF + 1 - f) // 2 + g - f - 1


def kernel(**inputs):
    import numpy as np
    import concourse.bacc as bacc
    from concourse.bass_utils import run_bass_kernel_spmd

    ids = np.asarray(inputs["ids"])
    batch = ids.shape[0]
    w1 = np.asarray(inputs["W_top1"])
    w1_laid = np.zeros((NSTEP, P, H1), w1.dtype)
    for lo, hi, p in GROUPS:
        for b in range(lo, hi + 1):
            for a in range(b):
                w1_laid[b - lo, p + a] = w1[pair_row(*sorted((ORDER[a], ORDER[b])))]
    w1_laid[NSTEP - 1] = w1[NPAIR:]
    dense = np.asarray(inputs["r_dense_x"])
    arrays = {
        "ids": np.ascontiguousarray(ids[:, COLD].reshape(batch // P, P, NCOLD).transpose(1, 0, 2)),
        "ids_hot": np.ascontiguousarray(ids[:, HOT].T.reshape(P, NHOT * batch // P)),
        "dense": np.ascontiguousarray(dense),
        "dense_t": np.ascontiguousarray(dense.T),
        "w1": np.ascontiguousarray(w1_laid.transpose(1, 0, 2)),
        "b1": np.ascontiguousarray(np.asarray(inputs["b_top1"]).reshape(NH1, P).T),
        "w2": np.ascontiguousarray(np.asarray(inputs["W_top2"]).reshape(NH1, P, H2).transpose(1, 0, 2)),
        "b2": np.ascontiguousarray(np.asarray(inputs["b_top2"]).reshape(NH2, P).T),
        "w3": np.ascontiguousarray(np.asarray(inputs["W_top3"]).reshape(NH2, P).T),
        "ident": np.eye(P, dtype=np.float32),
        "limit": np.ascontiguousarray(np.broadcast_to(np.array([ROWS[f] for f in COLD], np.int32), (P, NCOLD))),
        "hot_row": np.arange(HROWS, dtype=np.int32).reshape(HP, NCH),
    }
    for f in range(NF):
        arrays[f"tbl_{f}"] = np.ascontiguousarray(inputs[f"tbl_{f}"])

    nc = bacc.Bacc("TRN2", target_bir_lowering=False, num_devices=1)
    ap = {name: nc.dram_tensor(name, a.shape, mybir.dt.from_np(a.dtype), kind="ExternalInput").ap()
          for name, a in arrays.items()}
    scratch = nc.dram_tensor("ids_scratch", (P, NHOT * batch // P), I32).ap()
    out = nc.dram_tensor("out", (P, batch // P), F32, kind="ExternalOutput").ap()
    tables = {f: ap[f"tbl_{f}"] for f in range(NF)}
    build(nc, ap["ids"], ap["ids_hot"], tables, [tables[f] for f in HOT], ap["dense"], ap["dense_t"],
          ap["w1"], ap["b1"], ap["w2"], ap["b2"], ap["w3"], ap["ident"], ap["limit"],
          ap["hot_row"], scratch, out)
    r = run_bass_kernel_spmd(nc, [arrays], core_ids=[0])
    return np.ascontiguousarray(r.results[0]["out"].T).reshape(batch, 1)
```

```python
from contextlib import ExitStack

import concourse.bass as bass
from concourse import mybir

F32 = mybir.dt.float32
F32R = mybir.dt.float32r
I32 = mybir.dt.int32
ALU = mybir.AluOpType
ACT = mybir.ActivationFunctionType

P = 128
ROWS = (1000, 1250, 125000, 1250, 1000, 1250, 12500, 1250, 12500, 12500, 12500, 12500, 1000,
        1250, 12500, 1250, 1250, 1000, 1000, 12500, 12500, 1000, 1250, 1250, 1250, 1000)
NF = len(ROWS)
NHOT = 8
HOT = sorted(range(NF), key=lambda f: (ROWS[f], f))[:NHOT]
COLD = [f for f in range(NF) if f not in HOT]
NCOLD = len(COLD)
ORDER = COLD + [NF] + HOT
HP = 125
NCH = [ROWS[f] // HP for f in HOT]
assert all(n * HP == ROWS[f] for n, f in zip(NCH, HOT))
CH0 = [sum(NCH[:t]) for t in range(NHOT + 1)]
NEARLY = 3
NSPLIT = 5
IN_W1 = range(NSPLIT, NHOT - 1)
FS = NF + 1
PER_BANK = 4
NGROUP = -(-(NCOLD + 1) // PER_BANK)
NQ = 4
QUAD = P // NQ
NSLOT = 2
NHB = 3
NPAIR = NF * (NF + 1) // 2
PSTEP = -(-NPAIR // P)
NSTEP = PSTEP + 1
H1, H2 = 512, 256
NH1, NH2 = H1 // P, H2 // P

HALF_0 = ("M0", "T0", "I0", "I1", "M1", "I2", "I3", "A", "T1", "O0", "Y", "T2", "O1", "O2", "T3", "O3", "O4",
          "T4")
FIRST_TURN = (("T0", "O0", "T1", "O1", "O2", "T2", "O3", "T3", "T4", "O4"),
              ("T0", "O5", "T1", "O6", "O7", "T2", "I0", "I1", "T3", "I2", "I3", "A", "T4"))
SECOND_TURN = (("O0", "I0", "I1", "T0", "I2", "I3", "A", "O1", "T1", "O2", "T2", "O3", "T3", "O4", "T4"),
               ("O5", "O6", "L0", "T0", "O7", "L1", "T1", "L2", "I0", "I1", "L3", "T2", "I2", "I3", "A", "T3",
               "T4"))
TURN = (HALF_0, ("L0", "T0", "O5", "O6", "L1", "T1", "O7", "T2", "L2", "I0", "I1", "T3", "L3", "I2", "I3", "A",
                "T4"))
LAST_TURN = (HALF_0, ("L0", "T0", "O5", "O6", "L1", "T1", "O7", "T2", "L2", "I0", "I1", "T3", "L3", "I2", "T4",
                     "I3", "A"),
             ("I0", "I1", "N0", "I2", "I3", "A", "N1", "Z", "F0", "F1", "F2", "F3", "G0", "G1", "H0", "H1",
              "H2", "H3", "K0", "K1", "X", "Y"))
NPIECE = 4


def pair_groups():
    groups, last, p = [], NF, 0
    while last > 0:
        first = max(1, last - PSTEP + 1)
        groups.append((first, last, p))
        p += last
        last = first - 1
    assert p <= P
    return groups


GROUPS = pair_groups()
NPOOL = 3


def fills_bank(step):
    return step[0] in "TO"


def build(nc, ids, ids_hot, tables, hot_tables, dense, dense_t, w1, b1, w2, b2, w3,
          ident, limit, hot_row, hot_limit, ids_scratch, out):
    batch = dense.shape[0]
    ntile = batch // P
    nblock = ntile // NSLOT
    BLK = NSLOT * P
    NHCOL = NHOT * batch // P
    plain = [(s, step) for s, half in enumerate(TURN) for step in half]
    opening = [(s, step) for s, half in enumerate(FIRST_TURN) for step in half]
    second = [(s, step) for s, half in enumerate(SECOND_TURN) for step in half]
    final = [(s, step) for s, half in enumerate(LAST_TURN) for step in half]

    def fills_of(body):
        return [b for b in body if fills_bank(b[1])]

    assert all(len(fills_of(body)) == 2 * NGROUP + NHOT for body in (opening, second, plain, final))

    with ExitStack() as ctx:
        def sb(name, shape, dt=F32):
            return ctx.enter_context(nc.sbuf_tensor(name, shape, dt))

        def psum(name, shape):
            return ctx.enter_context(nc.psum_tensor(name, shape, F32))

        def sem(name):
            return ctx.enter_context(nc.semaphore(name))

        ids_raw = sb("ids_raw", [P, ntile, NCOLD], I32)
        ids_neg = sb("ids_neg", [P, ntile, NCOLD], I32)
        ids_ok = sb("ids_ok", [P, ntile, NCOLD], I32)
        lim = sb("lim", [P, 2, NCOLD], I32)
        hot_raw = sb("hot_raw", [NHCOL, P], I32)
        hot_neg = sb("hot_neg", [NHCOL, P], I32)
        hot_ok = sb("hot_ok", [NHCOL, P], I32)
        hot_lim = sb("hot_lim", [NHCOL, 2])
        hrow = sb("hrow", [HP, CH0[NHOT]], I32)
        hot_ids = sb("hot_ids", [HP, NHOT, BLK], I32)
        idx = [sb(f"idx{s}", [P, NCOLD], I32) for s in range(NSLOT)]
        emb = [sb(f"emb{s}", [P, NCOLD + 1, P]) for s in range(NSLOT)]
        embT = sb("embT", [P, BLK, FS])
        dots = sb("dots", [P, NF * BLK])
        dots_v = dots[0:NF, :].rearrange("p (b s) -> p b s", b=NF)
        z = sb("z", [P, NSTEP, BLK])
        tab_hi = sb("tab_hi", [HP, CH0[NHOT], P], F32R)
        tab_lo = sb("tab_lo", [HP, CH0[NHOT], P], F32R)
        hot = [sb(f"hot{k}", [HP, max(NCH[k::NHB]), BLK], F32R) for k in range(NHB)]
        w1_sb = sb("w1_sb", [P, NSTEP, H1])
        w1_flat = w1_sb[:].rearrange("p k h -> p (k h)")

        def raw_tab(t):
            at = P * sum(NCH[u] for u in range(t) if (u in IN_W1) == (t in IN_W1))
            place, room = (w1_flat, NSTEP * H1) if t in IN_W1 else (dots, NF * BLK)
            assert at + NCH[t] * P <= room
            return place[0:HP, at:at + NCH[t] * P].rearrange("p (c d) -> p c d", d=P)

        w2_sb = sb("w2_sb", [P, NH1, H2])
        w3_sb = sb("w3_sb", [P, NH2])
        b1_sb = sb("b1_sb", [P, NH1])
        b2_sb = sb("b2_sb", [P, NH2])
        ident_sb = sb("ident_sb", [P, P])
        h1 = sb("h1", [P, NH1, BLK])
        h2 = sb("h2", [P, NH2, BLK])
        y = sb("y", [P, ntile])

        tp = [psum(f"tp{k}", [P, 512]) for k in range(2)]
        zp = [psum(f"zp{s}", [P, QUAD, 32]) for s in range(NSLOT)]
        hp = [psum(f"hp{k}", [P, 512]) for k in range(2)]

        ids_in = sem("ids_in")
        more_ids_in = sem("more_ids_in")
        hot_in = sem("hot_in")
        hrow_in = sem("hrow_in")
        ident_in = sem("ident_in")
        w_in = sem("w_in")
        table_in = [sem(f"table_in{t}") for t in range(NHOT)]
        table_hi = sem("table_hi")
        table_lo = sem("table_lo")
        clamped = sem("clamped")
        scratch_out = sem("scratch_out")
        z_zero = sem("z_zero")
        hot_ids_in = sem("hot_ids_in")
        idx_ready = [sem(f"idx_ready{s}") for s in range(NSLOT)]
        gathered = [[sem(f"gathered{s}_{g}") for g in range(NGROUP)] for s in range(NSLOT)]
        dense_in = [sem(f"dense_in{s}") for s in range(NSLOT)]
        tile_read = [sem(f"tile_read{s}") for s in range(NSLOT)]
        bank_full = [sem(f"bank_full{k}") for k in range(2)]
        bank_free = [sem(f"bank_free{k}") for k in range(2)]
        hot_made = sem("hot_made")
        hot_done = sem("hot_done")
        interacted = [sem(f"interacted{s}") for s in range(NSLOT)]
        dots_v_out = [sem(f"dots_by_vector{s}") for s in range(NSLOT)]
        dots_s_out = [sem(f"dots_by_scalar{s}") for s in range(NSLOT)]
        z_in = [sem(f"z_in{s}") for s in range(NSLOT)]
        z_in_pool = [sem(f"z_in_by_pool{s}") for s in range(NSLOT)]
        h1_full = sem("h1_full")
        h1_ready = sem("h1_ready")
        h2_full = sem("h2_full")
        h2_ready = sem("h2_ready")
        y_full = sem("y_full")
        y_ready = sem("y_ready")
        stored = sem("stored")

        def members(g):
            return range(PER_BANK * g, min(PER_BANK * (g + 1), NCOLD + 1))

        def cold_members(g):
            return sum(f < NCOLD for f in members(g))

        def on_bank_full(step):
            return step[0] == "T" and step != f"T{NGROUP - 1}"

        def fill_number(body, s, step):
            return fills_of(body).index((s, step))

        def bank_of(body, s, step):
            return fill_number(body, s, step) % 2

        def freed_before(body, s, step):
            return fill_number(body, s, step) // 2

        FREED = [(2 * NGROUP + NHOT + 1 - k) // 2 for k in range(2)]

        def full_upto(body, s, step):
            n = fill_number(body, s, step)
            return sum(m % 2 == n % 2 and on_bank_full(f) for m, (_, f) in enumerate(fills_of(body)[:n + 1]))

        def full_per_turn(k, body=plain):
            return sum(m % 2 == k and on_bank_full(f) for m, (_, f) in enumerate(fills_of(body)))

        def full_before(body, k, i):
            if body is opening:
                return 0
            if body is second:
                return full_per_turn(k, opening)
            extra = sum(full_per_turn(k, b) - full_per_turn(k) for b in (opening, second))
            return i * full_per_turn(k) + extra

        Z_MOVES = (len(GROUPS) + 1, len(GROUPS))

        def z_part(lo, hi, p, s):
            return z[p:p + hi, 0:hi - lo + 1, P * s:P * (s + 1)]

        def dots_part(lo, hi, s):
            return dots_v[0:hi, lo - 1:hi, P * s:P * (s + 1)]

        dense_v = dense.rearrange("(t p) d -> t p d", p=P)
        block = ctx.enter_context(nc.Block())

        @block.sync
        def _(sp):
            sp.dma_start(ids_raw[:, 0:1, :], ids[:, 0:1, :]).then_inc(ids_in, 16)
            sp.dma_start(hot_raw[:], ids_hot).then_inc(hot_in, 16)
            sp.dma_start(ids_raw[:, 1:, :], ids[:, 1:, :]).then_inc(more_ids_in, 16)
            sp.dma_start(ident_sb[:], ident).then_inc(ident_in, 16)
            sp.dma_start(hrow[:], hot_row).then_inc(hrow_in, 16)

            def load_dense(s, i):
                sp.dma_start(emb[s][:, NCOLD, :], dense_v[i * NSLOT + s, :, :]).then_inc(dense_in[s], 16)

            def load_hot_ids(i):
                src = ids_scratch.rearrange("(t q) n -> t (q n)", t=NHOT)[:, bass.ds(i * BLK, BLK)]
                sp.dma_start(hot_ids[:], src[None, :, :].broadcast_to([HP, NHOT, BLK])
                             ).then_inc(hot_ids_in, 16)

            def move_dots(s, j, first=False, groups=GROUPS):
                if s == 0 and not first:
                    sp.wait_ge(h1_full, j * NH1)
                if s == 0:
                    sp.dma_start(z[:, NSTEP - 1, :], dense_t[:, bass.ds(j * BLK, BLK)]).then_inc(z_in[s], 16)
                sp.wait_ge(dots_v_out[s], j + 1)
                sp.wait_ge(dots_s_out[s], j + 1)
                for lo, hi, p in groups:
                    sp.dma_start(z_part(lo, hi, p, s), dots_part(lo, hi, s)).then_inc(z_in[s], 16)

            def turn(i, first=False, last=False):
                if not first:
                    move_dots(1, i - 1)
                if not last:
                    sp.wait_ge(hot_made, i * NHOT + NHOT)
                    load_hot_ids(i + 1)
                    sp.wait_ge(tile_read[0], i + 1)
                    load_dense(0, i + 1)
                if first:
                    sp.wait_ge(z_zero, 1)
                move_dots(0, i, first, GROUPS[NPOOL:] if last else GROUPS)
                if not last:
                    sp.wait_ge(tile_read[1], i + 1)
                    load_dense(1, i + 1)

            sp.wait_ge(clamped, 6)
            sp.dma_start(ids_scratch, hot_ok[:]).then_inc(scratch_out, 16)
            sp.wait_ge(scratch_out, 16)
            load_hot_ids(0)
            for s in range(NSLOT):
                load_dense(s, 0)
            sp.wait_ge(table_lo, NHOT)
            for here, there in ((w1_sb, w1), (w2_sb, w2), (w3_sb, w3), (b1_sb, b1), (b2_sb, b2)):
                sp.dma_start(here[:], there).then_inc(w_in, 16)
            turn(0, first=True)
            with nc.sync.Fori(1, nblock - 1) as i:
                turn(i)
            turn(nblock - 1, last=True)
            move_dots(1, nblock - 1, groups=GROUPS[NPOOL:])
            sp.wait_ge(y_ready, nblock)
            sp.dma_start(out, y[:]).then_inc(stored, 16)
            sp.wait_ge(stored, 16)

        @block.gpsimd
        def _(pool):
            with nc.gpsimd.Fori(1, nblock + 1) as turn:
                for s in range(NSLOT):
                    pool.wait_ge(ids_in, 32)
                    pool.wait_ge(idx_ready[s], turn)
                    for n in range(NCOLD):
                        nc.gpsimd.indirect_dma_start(
                            emb[s][:, n, :], None, tables[COLD[n]],
                            bass.IndirectOffsetOnAxis(idx[s][:, n:n + 1], 0),
                        ).then_inc(gathered[s][n // PER_BANK], 16)
            for s in range(NSLOT):
                if s == 0:
                    pool.wait_ge(h1_full, (nblock - 1) * NH1)
                pool.wait_ge(dots_v_out[s], nblock)
                pool.wait_ge(dots_s_out[s], nblock)
                for lo, hi, p in GROUPS[0:NPOOL]:
                    pool.dma_start(z_part(lo, hi, p, s), dots_part(lo, hi, s)).then_inc(z_in_pool[s], 16)

        def dots_copy(copy, s, c):
            return copy(dots_v[:, :, P * s + QUAD * c:P * s + QUAD * (c + 1)],
                        zp[s][32 * c:32 * c + NF, :, 0:NF].rearrange("a u b -> a b u"))

        @block.scalar
        def _(act):
            act.dma_start(lim[:], limit).then_inc(ids_in, 16)
            act.dma_start(hot_lim[:], hot_limit).then_inc(hot_in, 16)

            def load_table(t):
                act.dma_start(raw_tab(t), hot_tables[t].rearrange("(p c) d -> p c d", c=NCH[t])
                              ).then_inc(table_in[t], 16)

            def make_high(t):
                act.wait_ge(table_in[t], 16)
                nc.scalar.copy(tab_hi[:, CH0[t]:CH0[t + 1], :], raw_tab(t)).then_inc(table_hi, 1)

            for t in range(NEARLY):
                load_table(t)
            act.wait_ge(clamped, 6)
            load_table(NEARLY)
            for t in range(NEARLY):
                make_high(t)
            act.wait_ge(scratch_out, 16)
            for t in range(NEARLY + 1, NHOT):
                load_table(t)
            for t in range(NEARLY, NSPLIT):
                make_high(t)

            def embT_cols(s, lo, hi):
                return embT[:, P * s:P * (s + 1), lo:hi].rearrange("d b f -> d f b")

            def empty_bank(body, s, step, i, first):
                k = bank_of(body, s, step)
                n = int(step[1:])
                if first and step == "O0":
                    for t in range(NSPLIT, NHOT):
                        make_high(t)
                if step[0] == "O":
                    act.wait_ge(hot_done, i * NHOT + (n + 1))
                elif on_bank_full(step):
                    act.wait_ge(bank_full[k], full_before(body, k, i) + full_upto(body, s, step))
                else:
                    act.wait_ge(tile_read[s], i + 1)
                if step[0] == "T":
                    if n == 0 and not first:
                        act.wait_ge(interacted[s], i)
                    m = members(n)
                    src = tp[k][:, 0:P * len(m)].rearrange("d (f b) -> d f b", b=P)
                    nc.scalar.copy(embT_cols(s, m[0], m[-1] + 1), src).then_inc(bank_free[k], 1)
                else:
                    if n == 0 and not first:
                        act.wait_ge(interacted[1], i)
                    nc.scalar.copy(embT[:, :, NCOLD + 1 + n], tp[k][:, 0:BLK]).then_inc(bank_free[k], 1)

            def copy_dots(s, j, first=False):
                if first:
                    act.wait_ge(table_lo, NHOT)
                act.wait_ge(interacted[s], j + 1)
                dots_copy(nc.scalar.copy, s, 2)
                dots_copy(nc.scalar.copy, s, 3).then_inc(dots_s_out[s], 1)

            def first_layer(m, before, cols=slice(0, BLK)):
                act.wait_ge(h1_full, before + (m + 1))
                nc.scalar.activation(h1[:, m, cols], hp[m % 2][:, cols], ACT.Relu,
                                     bias=b1_sb[:, m:m + 1]).then_inc(h1_ready, 1)

            def second_layer(n, before, cols=slice(0, BLK), banks=hp):
                act.wait_ge(h2_full, before + (n + 1))
                nc.scalar.activation(h2[:, n, cols], banks[n % 2][:, cols], ACT.Relu,
                                     bias=b2_sb[:, n:n + 1]).then_inc(h2_ready, 1)

            def output(j):
                act.wait_ge(y_full, j + 1)
                nc.scalar.copy(y[:, bass.ds(j * NSLOT, NSLOT)], hp[0][:, 0:NSLOT]).then_inc(y_ready, 1)

            def turn(i, past=2, body=plain):
                for s, step in body:
                    n = int(step[1:] or 0)
                    if fills_bank(step):
                        empty_bank(body, s, step, i, past == 0)
                    elif step == "A" and s == 0 and past >= 1:
                        copy_dots(1, i - 1)
                    elif step == "A" and s == 1:
                        copy_dots(0, i, past == 0)
                    elif step[0] == "L" and past >= 1:
                        first_layer(n, (i - 1) * NH1)
                    elif step[0] == "M" and past >= 2:
                        second_layer(n, (i - 2) * NH2)
                    elif step == "Y" and past >= 2:
                        output(i if s == 2 else i - 2)
                    elif step[0] == "N":
                        second_layer(n, (i - 1) * NH2)
                    elif step == "Z":
                        output(i - 1)
                    elif step == "A" and s == 2:
                        copy_dots(1, i)
                    elif step[0] in "FH":
                        k = "FH".index(step[0])
                        first_layer(n, (i + k) * NH1, slice(P * k, P * (k + 1)))
                    elif step[0] in "GK":
                        k = "GK".index(step[0])
                        second_layer(n, (i + k) * NH2, slice(P * k, P * (k + 1)), tp)

            turn(0, past=0, body=opening)
            turn(1, past=1, body=second)
            with nc.scalar.Fori(2, nblock - 1) as i:
                turn(i)
            turn(nblock - 1, body=final)

        @block.vector
        def _(dve):
            def clamp_ids(tiles, done):
                rows, top = (lim[:, k:k + 1, :].broadcast_to([P, tiles.stop - tiles.start, NCOLD]) for k in range(2))
                nc.vector.scalar_tensor_tensor(out=ids_neg[:, tiles, :], in0=ids_raw[:, tiles, :], scalar=0, in1=rows,
                                               op0=ALU.is_lt, op1=ALU.mult).then_inc(clamped, 1)
                dve.wait_ge(clamped, done + 1)
                nc.vector.tensor_tensor(ids_neg[:, tiles, :], ids_raw[:, tiles, :], ids_neg[:, tiles, :], ALU.add
                                        ).then_inc(clamped, 1)
                dve.wait_ge(clamped, done + 2)
                nc.vector.scalar_tensor_tensor(out=ids_ok[:, tiles, :], in0=ids_neg[:, tiles, :], scalar=0, in1=top,
                                               op0=ALU.max, op1=ALU.min).then_inc(clamped, 1)
                dve.wait_ge(clamped, done + 3)

            def stage_indices(s, i):
                nc.vector.tensor_copy(idx[s][:], ids_ok[:, bass.ds(i * NSLOT + s, 1), :]
                                      ).then_inc(idx_ready[s], 1)

            dve.wait_ge(ids_in, 32)
            clamp_ids(slice(0, 1), 0)
            stage_indices(0, 0)
            dve.wait_ge(hot_in, 32)
            nc.vector.tensor_scalar(hot_neg[:], hot_raw[:], 0, hot_lim[:, 0:1], ALU.is_lt, ALU.mult
                                    ).then_inc(clamped, 1)
            dve.wait_ge(clamped, 4)
            nc.vector.tensor_tensor(hot_neg[:], hot_raw[:], hot_neg[:], ALU.add).then_inc(clamped, 1)
            dve.wait_ge(clamped, 5)
            nc.vector.tensor_scalar(hot_ok[:], hot_neg[:], hot_lim[:, 1:2], 0, ALU.min, ALU.max
                                    ).then_inc(clamped, 1)
            dve.wait_ge(more_ids_in, 16)
            clamp_ids(slice(1, ntile), 6)
            stage_indices(1, 0)
            nc.vector.memset(z[:], 0.0).then_inc(z_zero, 1)
            dve.wait_ge(hrow_in, 16)

            def make_low(t):
                dve.wait_ge(table_hi, t + 1)
                chunks = slice(CH0[t], CH0[t + 1])
                nc.vector.tensor_tensor(tab_lo[:, chunks, :], raw_tab(t), tab_hi[:, chunks, :].bitcast(F32),
                                        ALU.subtract).then_inc(table_lo, 1)

            def make_hot(t, i, first=False):
                if t == 0:
                    dve.wait_ge(hot_ids_in, i * 16 + 16)
                if t >= NHB:
                    dve.wait_ge(hot_done, i * NHOT + (t - NHB + 1))
                elif not first:
                    dve.wait_ge(hot_done, i * NHOT - (NHOT - 1 - max(range(t, NHOT, NHB))))
                shape = [HP, NCH[t], BLK]
                nc.vector.tensor_tensor(hot[t % NHB][:, 0:NCH[t], :],
                                        hot_ids[:, t:t + 1, :].broadcast_to(shape),
                                        hrow[:, CH0[t]:CH0[t + 1], None].broadcast_to(shape),
                                        ALU.is_equal).then_inc(hot_made, 1)

            def copy_dots(s, j):
                dve.wait_ge(interacted[s], j + 1)
                dots_copy(nc.vector.tensor_copy, s, 0)
                dots_copy(nc.vector.tensor_copy, s, 1).then_inc(dots_v_out[s], 1)

            def turn(i, second=False, last=False):
                done = NHB + 1 if second else NHB
                for t in range(1 if second else 0, done):
                    make_hot(t, i)
                copy_dots(1, i - 1)
                for t in range(done, NHOT):
                    make_hot(t, i)
                if not last:
                    dve.wait_ge(tile_read[0], i + 1)
                    stage_indices(0, i + 1)
                copy_dots(0, i)
                if not last:
                    dve.wait_ge(tile_read[1], i + 1)
                    stage_indices(1, i + 1)

            for t in range(NEARLY):
                make_low(t)
            for t in range(NHOT):
                make_hot(t, 0, first=True)
                if t + NEARLY < NHOT:
                    make_low(t + NEARLY)
                if t == NSPLIT:
                    dve.wait_ge(tile_read[0], 1)
                    stage_indices(0, 1)
            make_hot(0, 1)
            dve.wait_ge(table_lo, NHOT)
            copy_dots(0, 0)
            dve.wait_ge(tile_read[1], 1)
            stage_indices(1, 1)
            turn(1, second=True)
            with nc.vector.Fori(2, nblock - 1) as i:
                turn(i)
            turn(nblock - 1, last=True)
            copy_dots(1, nblock - 1)

        @block.tensor
        def _(pe):
            def wait_bank(body, s, step, i, first):
                k, n = bank_of(body, s, step), freed_before(body, s, step)
                if not first or n:
                    pe.wait_ge(bank_free[k], i * FREED[k] + n)

            def transpose_group(body, s, step, i, first):
                k, g = bank_of(body, s, step), int(step[1:])
                m = members(g)
                if cold := 16 * cold_members(g):
                    pe.wait_ge(gathered[s][g], i * cold + cold)
                if m[-1] == NCOLD:
                    pe.wait_ge(dense_in[s], i * 16 + 16)
                wait_bank(body, s, step, i, first)
                for f in m:
                    n = f - m[0]
                    last = nc.tensor.transpose(tp[k][:, P * n:P * (n + 1)], emb[s][:, f, :], ident_sb[:])
                last.then_inc(bank_full[k] if on_bank_full(step) else tile_read[s], 1)

            def hot_product(body, s, step, i, first):
                k, t = bank_of(body, s, step), int(step[1:])
                pe.wait_ge(hot_made, i * NHOT + (t + 1))
                if first:
                    pe.wait_ge(table_lo, t + 1)
                wait_bank(body, s, step, i, first)
                for c in range(NCH[t]):
                    for tab in (tab_hi, tab_lo):
                        last = nc.tensor.matmul(tp[k][:, 0:BLK], tab[:, CH0[t] + c, :], hot[t % NHB][:, c, :],
                                                start=(c == 0 and tab is tab_hi),
                                                stop=(c == NCH[t] - 1 and tab is tab_lo))
                last.then_inc(hot_done, 1)

            def interact(body, s, piece, j, first=False):
                if piece == 0:
                    for k in range(2):
                        last = max(n for n, fill in enumerate(fills_of(body)) if n % 2 == k
                                   and (fill[0] == s or fill[1][0] == "O"))
                        pe.wait_ge(bank_free[k], j * FREED[k] + last // 2 + 1)
                    if not first:
                        pe.wait_ge(dots_v_out[s], j)
                        pe.wait_ge(dots_s_out[s], j)
                n = QUAD // NPIECE
                for u in range(n * piece, n * (piece + 1)):
                    for c in range(NQ):
                        b = P * s + QUAD * c + u
                        last = nc.tensor.matmul(zp[s][32 * c:32 * c + NF, u, 0:NF],
                                                embT[:, b, 0:NF], embT[:, b, 1:NF + 1],
                                                start=True, stop=True)
                if piece == NPIECE - 1:
                    last.then_inc(interacted[s], 1)

            def first_layer(m, before, cols=slice(0, BLK)):
                if m >= 2:
                    pe.wait_ge(h1_ready, before + (m - 1))
                for k in range(NSTEP):
                    last = nc.tensor.matmul(hp[m % 2][:, cols], w1_sb[:, k, P * m:P * (m + 1)],
                                            z[:, k, cols], start=(k == 0), stop=(k == NSTEP - 1))
                last.then_inc(h1_full, 1)

            def second_layer(n, before, h1_before, cols=slice(0, BLK), banks=hp):
                if n == 0 and banks is hp:
                    pe.wait_ge(h1_ready, h1_before + NH1)
                for m in range(NH1):
                    if n == 0 and banks is tp:
                        pe.wait_ge(h1_ready, h1_before + m + 1)
                    last = nc.tensor.matmul(banks[n % 2][:, cols], w2_sb[:, m, P * n:P * (n + 1)],
                                            h1[:, m, cols], start=(m == 0), stop=(m == NH1 - 1))
                last.then_inc(h2_full, 1)

            def output(h2_before, s_from=0, s_to=NSLOT):
                pe.wait_ge(h2_ready, h2_before + NH2)
                for s in range(s_from, s_to):
                    for n in range(NH2):
                        last = nc.tensor.matmul(hp[0][:, s:s + 1], h2[:, n, P * s:P * (s + 1)],
                                                w3_sb[:, n:n + 1], start=(n == 0), stop=(n == NH2 - 1))
                if s_to == NSLOT:
                    last.then_inc(y_full, 1)

            def pairs_in(s, j, last=False):
                if not last:
                    pe.wait_ge(z_in[s], j * (16 * Z_MOVES[s]) + 16 * Z_MOVES[s])
                else:
                    pe.wait_ge(z_in[s], j * (16 * Z_MOVES[s]) + 16 * (Z_MOVES[s] - NPOOL))
                    pe.wait_ge(z_in_pool[s], 16 * NPOOL)

            def turn(i, past=2, body=plain):
                for s, step in body:
                    n = int(step[1:] or 0)
                    if step[0] == "T":
                        transpose_group(body, s, step, i, past == 0)
                    elif step[0] == "O":
                        hot_product(body, s, step, i, past == 0)
                    elif step[0] == "I" and s == 0 and past >= 1:
                        interact(body, 1, n, i - 1, past == 1)
                    elif step[0] == "I" and s == 1:
                        interact(body, 0, n, i, past == 0)
                    elif step[0] == "L" and past >= 1:
                        if n == 0:
                            for k in range(NSLOT):
                                pairs_in(k, i - 1)
                            if past >= 2:
                                pe.wait_ge(y_ready, i - 1)
                        first_layer(n, (i - 1) * NH1)
                    elif step[0] == "M" and past >= 2:
                        second_layer(n, (i - 2) * NH2, (i - 2) * NH1)
                    elif step == "X":
                        pe.wait_ge(h1_ready, (i + 2) * NH1)
                        output(i * NH2, 0, 1)
                    elif step == "Y" and s == 2:
                        output((i + 1) * NH2, 1)
                    elif step == "Y" and past >= 2:
                        output((i - 2) * NH2)
                    elif step[0] == "N":
                        second_layer(n, (i - 1) * NH2, (i - 1) * NH1)
                    elif step == "Z":
                        output((i - 1) * NH2)
                    elif step[0] == "I" and s == 2:
                        interact(body, 1, n, i)
                    elif step[0] in "FH":
                        k = "FH".index(step[0])
                        if k == 1 and n < 2:
                            pe.wait_ge(h1_ready, (i + 1) * NH1 - (1 - n))
                        if n == 0:
                            if k == 0:
                                pe.wait_ge(y_ready, i)
                            pairs_in(k, i, last=True)
                        first_layer(n, (i + k) * NH1, slice(P * k, P * (k + 1)))
                    elif step[0] in "GK":
                        k = "GK".index(step[0])
                        if k == 1 and n == 0:
                            pe.wait_ge(h2_ready, (i + 1) * NH2)
                        second_layer(n, (i + k) * NH2, (i + k) * NH1, slice(P * k, P * (k + 1)), tp)

            pe.wait_ge(ident_in, 16)
            turn(0, past=0, body=opening)
            pe.wait_ge(w_in, 80)
            turn(1, past=1, body=second)
            with nc.tensor.Fori(2, nblock - 1) as i:
                turn(i)
            turn(nblock - 1, body=final)


def pair_row(f, g):
    return f * (2 * NF + 1 - f) // 2 + g - f - 1


def kernel(**inputs):
    import numpy as np
    import concourse.bacc as bacc
    from concourse.bass_utils import run_bass_kernel_spmd

    ids = np.asarray(inputs["ids"])
    batch = ids.shape[0]
    w1 = np.asarray(inputs["W_top1"])
    w1_laid = np.zeros((NSTEP, P, H1), w1.dtype)
    for lo, hi, p in GROUPS:
        for b in range(lo, hi + 1):
            for a in range(b):
                w1_laid[b - lo, p + a] = w1[pair_row(*sorted((ORDER[a], ORDER[b])))]
    w1_laid[NSTEP - 1] = w1[NPAIR:]
    dense = np.asarray(inputs["r_dense_x"])
    arrays = {
        "ids": np.ascontiguousarray(ids[:, COLD].reshape(batch // P, P, NCOLD).transpose(1, 0, 2)),
        "ids_hot": np.ascontiguousarray(ids[:, HOT].T.reshape(NHOT * batch // P, P)),
        "dense": np.ascontiguousarray(dense),
        "dense_t": np.ascontiguousarray(dense.T),
        "w1": np.ascontiguousarray(w1_laid.transpose(1, 0, 2)),
        "b1": np.ascontiguousarray(np.asarray(inputs["b_top1"]).reshape(NH1, P).T),
        "w2": np.ascontiguousarray(np.asarray(inputs["W_top2"]).reshape(NH1, P, H2).transpose(1, 0, 2)),
        "b2": np.ascontiguousarray(np.asarray(inputs["b_top2"]).reshape(NH2, P).T),
        "w3": np.ascontiguousarray(np.asarray(inputs["W_top3"]).reshape(NH2, P).T),
        "ident": np.eye(P, dtype=np.float32),
        "limit": np.ascontiguousarray(np.broadcast_to(
            np.array([[ROWS[f] for f in COLD], [ROWS[f] - 1 for f in COLD]], np.int32), (P, 2, NCOLD))),
        "hot_row": np.concatenate([np.arange(ROWS[f], dtype=np.int32).reshape(HP, -1) for f in HOT], axis=1),
        "hot_limit": np.repeat(np.array([[ROWS[f], ROWS[f] - 1] for f in HOT], np.float32), batch // P, axis=0),
    }
    for f in range(NF):
        arrays[f"tbl_{f}"] = np.ascontiguousarray(inputs[f"tbl_{f}"])

    nc = bacc.Bacc("TRN2", target_bir_lowering=False, num_devices=1)
    ap = {name: nc.dram_tensor(name, a.shape, mybir.dt.from_np(a.dtype), kind="ExternalInput").ap()
          for name, a in arrays.items()}
    scratch = nc.dram_tensor("ids_scratch", (NHOT * batch // P, P), I32).ap()
    out = nc.dram_tensor("out", (P, batch // P), F32, kind="ExternalOutput").ap()
    tables = {f: ap[f"tbl_{f}"] for f in range(NF)}
    build(nc, ap["ids"], ap["ids_hot"], tables, [tables[f] for f in HOT], ap["dense"], ap["dense_t"],
          ap["w1"], ap["b1"], ap["w2"], ap["b2"], ap["w3"], ap["ident"], ap["limit"],
          ap["hot_row"], ap["hot_limit"], scratch, out)
    r = run_bass_kernel_spmd(nc, [arrays], core_ids=[0])
    return np.ascontiguousarray(r.results[0]["out"].T).reshape(batch, 1)
```
